# Optimizing a Trainium2 kernel written in Bass

```python
import numpy as np
import jax
import jax.numpy as jnp

def _softmax(x, axis=-1):
    return jax.nn.softmax(x, axis=axis)

def _gelu(x):
    return jax.nn.gelu(x, approximate=True)

def _silu(x):
    return jax.nn.silu(x)

def _sigmoid(x):
    return jax.nn.sigmoid(x)

def _layernorm(x, axis=-1, eps=1e-05):
    m = jnp.mean(x, axis=axis, keepdims=True)
    v = jnp.var(x, axis=axis, keepdims=True)
    return (x - m) / jnp.sqrt(v + eps)

def _scatter_add(tgt, idx, src, axis=0):
    return tgt.at[idx].add(src)

def _segment_sum(src, seg, n):
    return jax.ops.segment_sum(src, seg, n)
kernel_name = 'mk_adj_resnorm_d2_adj_r2_ae2b60'

def setup_inputs(seed: int=0):
    np.random.seed(seed)
    _w = jnp.asarray

    def _rec_inputs():
        import jax
        import jax.numpy as jnp
        _gk = jax.random.key(seed)
        x = -0.000929 + 1 * jax.random.normal(jax.random.fold_in(_gk, 1), (4096, 128), jnp.float32)
        _a = jax.random.bernoulli(jax.random.fold_in(_gk, 2), 0.00390625, (4096, 4096))
        _a = jnp.logical_or(_a, jnp.eye(4096, dtype=bool))
        _af = _a.astype(jnp.float32)
        _af = _af * jax.random.uniform(jax.random.fold_in(_gk, 3), (4096, 4096), jnp.float32, 0.05, 1)
        adj = _af
        return (x, adj)
    x, adj = _rec_inputs()

    def _L0_gnn_setup():
        import jax, jax.numpy as jnp
        import numpy as np
        N = 4096
        H = 128
        key = jax.random.key(seed)
        k_x, k_A, k_W = jax.random.split(key, 3)
        x = jax.random.normal(k_x, (N, H), dtype=jnp.float32)
        A = jax.random.uniform(k_A, (N, N), dtype=jnp.float32)
        alpha = jnp.array([0.5], dtype=jnp.float32)
        bound = 1.0 / np.sqrt(H)
        W = jax.random.uniform(k_W, (H, H), dtype=jnp.float32, minval=-bound, maxval=bound)
        b = jnp.zeros((H,), dtype=jnp.float32)
        t = jnp.zeros((1,), dtype=jnp.float32)
        return {'t': t, 'x': x, 'A': A, 'alpha': alpha, 'W': W, 'b': b}
    _L0_gnn_all = _L0_gnn_setup()
    _L0_gnn_in = {k: v for k, v in _L0_gnn_all.items() if k in ('t', 'alpha', 'W', 'b')}
    del _L0_gnn_all

    def _L1_gnn_setup():
        import jax, jax.numpy as jnp
        import numpy as np
        K = 5
        TAU = 0.5
        N = 4096
        IN_DIM = 128
        OUT_DIM = 128

        def _cheb_coeff(k_order: int, tau: float) -> jnp.ndarray:
            ks = jnp.arange(k_order, dtype=jnp.float32)
            x_k = jnp.cos(jnp.pi * (ks + 0.5) / k_order)
            return 2.0 / k_order * jnp.exp(-tau * x_k)
        key = jax.random.key(seed)
        k1, k2, k3 = jax.random.split(key, 3)
        x = jax.random.normal(k1, (N, IN_DIM), dtype=jnp.float32)
        laplacian = jax.random.normal(k2, (N, N), dtype=jnp.float32) / np.sqrt(N)
        limit = np.sqrt(6.0 / (IN_DIM + OUT_DIM))
        theta = jax.random.uniform(k3, (K, IN_DIM, OUT_DIM), dtype=jnp.float32, minval=-limit, maxval=limit)
        return {'x': x, 'laplacian': laplacian, 'theta': theta}
    _L1_gnn_all = _L1_gnn_setup()
    _L1_gnn_in = {k: v for k, v in _L1_gnn_all.items() if k in ('theta',)}
    del _L1_gnn_all
    return {'x': x, 'adj': adj, 'L0_gnn_t': _L0_gnn_in['t'], 'L0_gnn_alpha': _L0_gnn_in['alpha'], 'L0_gnn_W': _L0_gnn_in['W'], 'L0_gnn_b': _L0_gnn_in['b'], 'L1_gnn_theta': _L1_gnn_in['theta']}

def reference(x, adj, L0_gnn_t, L0_gnn_alpha, L0_gnn_W, L0_gnn_b, L1_gnn_theta):
    import jax
    import jax.numpy as jnp

    def _L0_gnn_ref(t, x, A, alpha, W, b):
        import jax, jax.numpy as jnp
        import numpy as np
        N = 4096
        H = 128
        a = alpha[0]
        A_prime = a * A
        diag = jnp.diagonal(A_prime) + (1.0 - a)
        A_prime = A_prime.at[jnp.arange(N), jnp.arange(N)].set(diag)
        out_degree = A_prime.sum(axis=1)
        inv_deg = jnp.where(out_degree == 0.0, 0.0, 1.0 / out_degree)
        x = inv_deg[:, None] * A_prime @ x
        x = x @ W.T + b
        return jax.nn.relu(x)

    def _L1_gnn_ref(x, laplacian, theta):
        import jax, jax.numpy as jnp
        import numpy as np
        K = 5
        TAU = 0.5
        N = 4096
        IN_DIM = 128
        OUT_DIM = 128

        def _cheb_coeff(k_order: int, tau: float) -> jnp.ndarray:
            ks = jnp.arange(k_order, dtype=jnp.float32)
            x_k = jnp.cos(jnp.pi * (ks + 0.5) / k_order)
            return 2.0 / k_order * jnp.exp(-tau * x_k)
        coeff = _cheb_coeff(K, TAU)
        tx_prev, tx_curr = (x, laplacian @ x)
        tx_list = [tx_prev, tx_curr]
        for _ in range(2, K):
            tx_next = 2.0 * (laplacian @ tx_curr) - tx_prev
            tx_list.append(tx_next)
            tx_prev, tx_curr = (tx_curr, tx_next)
        tx_stack = jnp.stack(tx_list, axis=0)
        return jnp.einsum('kni,kio,k->no', tx_stack, theta, coeff)
    x = _layernorm(x + _L0_gnn_ref(L0_gnn_t, x, adj, L0_gnn_alpha, L0_gnn_W, L0_gnn_b), axis=-1)
    x = _layernorm(x + _L1_gnn_ref(x, adj, L1_gnn_theta), axis=-1)
    return x

_drawn_inputs = setup_inputs


def setup_inputs(seed=0):
    import zlib

    import numpy as np

    out = dict(_drawn_inputs(seed))
    spreads = {'L0_gnn_b': (0.0, 0.1)}
    factors = {}
    for name, (base, spread) in spreads.items():
        noise = np.random.default_rng([zlib.crc32(name.encode()), seed]).standard_normal(out[name].shape)
        drawn = base * np.exp(spread * noise) if base else spread * noise
        out[name] = jnp.asarray(drawn.astype(out[name].dtype))
    for name, factor in factors.items():
        out[name] = (out[name] * factor).astype(out[name].dtype)
    return out
```

```python
from contextlib import ExitStack

import numpy as np

import concourse.bass as bass
from concourse import mybir

ALU = mybir.AluOpType
ACT = mybir.ActivationFunctionType
F32 = mybir.dt.float32
F32R = mybir.dt.float32r

P = 128
N = 4096
BLK = 512
NB = N // BLK
MT = BLK // P
K = 5
SWEEPS = K
RAW_SLOTS = 3
SPLIT_SLOTS = 3
EPS = 1e-5
TAU = 0.5
COEFF = [float(2.0 / K * np.exp(-TAU * np.cos(np.pi * (k + 0.5) / K))) for k in range(K)]


def plan_blocks():
    blocks, steps = [], []
    for s in range(SWEEPS):
        rows = range(NB) if s % 2 == 0 else range(NB - 1, -1, -1)
        for n in rows:
            before = list(range(n)) if s % 2 == 0 else list(range(NB - 1, n, -1))
            once = list(range(n, NB)) if s == 0 else [n]
            twice = before if s < SWEEPS - 1 else []
            if s == SWEEPS - 1:
                once = once + before
            first = len(blocks)
            g = len(steps)
            blocks += [dict(s=s, g=g, n=n, m=m, twice=False) for m in once]
            blocks += [dict(s=s, g=g, n=n, m=m, twice=True) for m in twice]
            steps.append(dict(s=s, g=g, n=n, first=first, last=len(blocks) - 1, once=len(once), twice=len(twice)))
    return blocks, steps


def plan_order(blocks, steps):
    made_by = {(st["s"] + 1, st["n"]): st["g"] for st in steps}
    order, pending = [], []
    pos = 0

    def flush(upto=None, key=None):
        while pending and (key is not None or pending[0][0] <= upto):
            item = pending.pop(0)[1]
            order.append(item)
            if item == key:
                break

    for st in steps:
        s, g = st["s"], st["g"]
        once = list(range(st["first"], st["first"] + st["once"]))
        twice = list(range(st["first"] + st["once"], st["last"] + 1))
        units = [("cur", i) for i in once]
        for q, i in enumerate(twice):
            units.append(("cur", i))
            if q >= 1:
                units.append(("next", twice[q - 1]))
        if twice:
            units.append(("next", twice[-1]))
        for unit in units:
            kind, i = unit
            j = s if kind == "cur" else s + 1
            if j >= 1:
                key = ("turn", made_by[(j, blocks[i]["m"])])
                if any(it == key for _, it in pending):
                    flush(key=key)
            flush(upto=pos)
            order.append(unit)
            pos += 1
            if unit == ("cur", st["last"]):
                if s == 0:
                    pending += [(pos + 1, ("w", g)), (pos + 3, ("norm", g)), (pos + 4, ("turn", g)), (pos + 5, ("theta", g))]
                elif s < SWEEPS - 1:
                    pending += [(pos + 1, ("turn", g)), (pos + 2, ("theta", g))]
                else:
                    pending += [(pos + 1, ("out", g)), (pos + 2, ("norm", g))]
    for _, item in pending:
        order.append(item)
    return order


def graph_layers(nc, a_blocks, x_nat, x_t, alpha, w_t, b, theta, out):
    blocks, steps = plan_blocks()
    order = plan_order(blocks, steps)
    made_by = {(st["s"] + 1, st["n"]): st["g"] for st in steps}
    part = {st["g"]: q for q, st in enumerate(x for x in steps if x["twice"])}
    sweep0 = [q for q, bl in enumerate(blocks) if bl["s"] == 0]
    FINAL = (SWEEPS - 1) * NB

    with ExitStack() as ctx:
        def sb(name, shape, dt=F32):
            return ctx.enter_context(nc.sbuf_tensor(name, shape, dt))

        def ps(name, shape):
            return ctx.enter_context(nc.psum_tensor(name, shape, F32))

        def sem(name):
            return ctx.enter_context(nc.semaphore(name))

        raw = sb("raw", [P, RAW_SLOTS, MT * BLK])
        a_hi = sb("a_hi", [P, SPLIT_SLOTS, MT * BLK], F32R)
        a_lo = sb("a_lo", [P, SPLIT_SLOTS, MT * BLK], F32R)
        v_hi = sb("v_hi", [P, 2, N], F32R)
        v_lo = sb("v_lo", [P, 2, N], F32R)
        vt = sb("vt", [P, 2, N])
        yt = sb("yt", [P, N])
        th = sb("th", [P, K, P])
        wt = sb("wt", [P, P])
        bb = sb("bb", [P, P])
        al = sb("al", [P, 2])
        ident = sb("ident", [P, P])
        ones = sb("ones", [P, 1])
        eps = sb("eps", [P, 1])
        sum_pool = sb("sum_pool", [P, 2, BLK])
        sum_dve = sb("sum_dve", [P, 2, BLK])
        zt = sb("zt", [P, BLK])
        pre = sb("pre", [P, BLK])
        nat = sb("nat", [P, 2, BLK])
        deg = sb("deg", [P, 5, MT])
        stats = sb("stats", [P, MT, 6])
        mv = sb("mv", [P, MT, 2])
        std = sb("std", [P, MT])
        rstd = sb("rstd", [P, MT])
        shift = sb("shift", [P, MT])

        p_cur = [ps(f"p_cur{q}", [P, BLK]) for q in range(2)]
        p_next = [ps(f"p_next{q}", [P, BLK]) for q in range(2)]
        p_turn = ps("p_turn", [P, BLK])
        p_theta = ps("p_theta", [P, BLK])
        p_rows = ps("p_rows", [P, BLK])
        p_deg = ps("p_deg", [P, MT])

        raw_in = [sem(f"raw_in{q}") for q in range(RAW_SLOTS)]
        x_in = [sem(f"x_in{c}") for c in range(NB)]
        xt_in, al_in, w_in, b_in, th_in = sem("xt_in"), sem("al_in"), sem("w_in"), sem("b_in"), sem("th_in")
        alpha_ready, consts_ready, zeroed, eps_ready = sem("alpha_ready"), sem("consts_ready"), sem("zeroed"), sem("eps_ready")
        theta_ready = sem("theta_ready")
        x_hi_ready, x_lo_ready, x_scaled = sem("x_hi_ready"), sem("x_lo_ready"), sem("x_scaled")
        hi_ready, lo_ready = sem("hi_ready"), sem("lo_ready")
        pool_summed, pool_chain = sem("pool_summed"), sem("pool_chain")
        dve_chain = sem("dve_chain")
        block_used = sem("block_used")
        cur_done = sem("cur_done")
        joined = sem("joined")
        part_kept = sem("part_kept")
        w_done, pre_read, var_ready, std_ready, rstd_ready, nat_ready = (
            sem("w_done"), sem("pre_read"), sem("var_ready"), sem("std_ready"), sem("rstd_ready"), sem("nat_ready"))
        turned, vt_copied = sem("turned"), sem("vt_copied")
        v_hi_ready, v_lo_ready = sem("v_hi_ready"), sem("v_lo_ready")
        theta_done, y_added = sem("theta_done"), sem("y_added")
        out_done, stored = sem("out_done"), [sem(f"stored{q}") for q in range(2)]

        def col(n):
            return slice(n * BLK, (n + 1) * BLK)

        def tile(n, t):
            return slice(n * BLK + t * P, n * BLK + (t + 1) * P)

        def t4(t):
            return slice(t * P, (t + 1) * P)

        def pool_tiles(i):
            return MT if blocks[i]["twice"] else MT - 1

        def ln_index(g):
            return g if g < NB else NB + g - FINAL

        block = ctx.enter_context(nc.Block())

        @block.sync
        def _(sp):
            for i, bl in enumerate(blocks):
                if i >= RAW_SLOTS:
                    sp.wait_ge(hi_ready, i - RAW_SLOTS + 1)
                    sp.wait_ge(lo_ready, i - RAW_SLOTS + 1)
                    sp.wait_ge(pool_summed, min(i - RAW_SLOTS + 1, len(sweep0)))
                sp.dma_start(raw[:, i % RAW_SLOTS, :], a_blocks[bl["n"], bl["m"]]).then_inc(raw_in[i % RAW_SLOTS], 16)

        @block.gpsimd
        def _(pool):
            chain = [0]

            def link(ins):
                chain[0] += 1
                ins.then_inc(pool_chain, 1)
                pool.wait_ge(pool_chain, chain[0])

            link(nc.gpsimd.memset(ident[:], 0.0))
            link(nc.gpsimd.affine_select(out=ident[:], in_=ident[:], compare_op=ALU.not_equal, fill=1.0, base=0,
                                         pattern=[[-1, P]], channel_multiplier=1))
            nc.gpsimd.memset(ones[:], 1.0).then_inc(consts_ready, 1)

            for i in sweep0:
                bl = blocks[i]
                k = bl["g"]
                acc = sum_pool[:, k % 2, :]
                pool.wait_ge(raw_in[i % RAW_SLOTS], 16 * (i // RAW_SLOTS + 1))
                if i == steps[k]["first"] and k >= 2:
                    pool.wait_ge(w_done, k - 1)
                tiles = [raw[:, i % RAW_SLOTS, t * BLK:(t + 1) * BLK] for t in range(pool_tiles(i))]
                if i == steps[k]["first"]:
                    link(nc.gpsimd.tensor_tensor(acc, tiles[0], tiles[1], ALU.add))
                    tiles = tiles[2:]
                for a in tiles[:-1]:
                    link(nc.gpsimd.tensor_tensor(acc, acc, a, ALU.add))
                nc.gpsimd.tensor_tensor(acc, acc, tiles[-1], ALU.add).then_inc(pool_summed, 1)
                pool.wait_ge(pool_summed, i + 1)

            for st in steps[FINAL:]:
                n, q = st["n"], ln_index(st["g"])
                pool.wait_ge(nat_ready, MT * (q + 1))
                pool.dma_start(out[n], nat[:, q % 2, :].rearrange("p (t f) -> p t f", t=MT)).then_inc(stored[q % 2], 16)
            for done in stored:
                pool.wait_ge(done, 16 * NB // 2)

        @block.scalar
        def _(act):
            for c in range(NB):
                act.dma_start(yt[:, col(c)], x_nat[c]).then_inc(x_in[c], 16)
                if c == 0:
                    act.dma_start(al[:, 0:1], alpha.to_broadcast([P, 1])).then_inc(al_in, 16)
            act.dma_start(vt[:, 0, :], x_t).then_inc(xt_in, 16)
            act.dma_start(wt[:], w_t).then_inc(w_in, 16)
            act.dma_start(bb[:], b.to_broadcast([P, P])).then_inc(b_in, 16)
            act.dma_start(th[:], theta).then_inc(th_in, 16)

            def split_hi(i):
                if i < NB:
                    act.wait_ge(x_in[i], 16)
                    nc.scalar.activation(v_hi[:, 0, col(i)], yt[:, col(i)], ACT.Copy).then_inc(x_hi_ready, 1)
                act.wait_ge(raw_in[i % RAW_SLOTS], 16 * (i // RAW_SLOTS + 1))
                if i >= SPLIT_SLOTS:
                    act.wait_ge(block_used, i - SPLIT_SLOTS + 1)
                nc.scalar.activation(a_hi[:, i % SPLIT_SLOTS, :], raw[:, i % RAW_SLOTS, :], ACT.Copy).then_inc(hi_ready, 1)

            def deviation(q):
                act.wait_ge(var_ready, q + 1)
                if q == 0:
                    act.wait_ge(eps_ready, 1)
                else:
                    act.wait_ge(rstd_ready, q)
                nc.scalar.activation(std[:], mv[:, :, 1], ACT.Sqrt, bias=eps[:]).then_inc(std_ready, 1)

            def normalise(q, src):
                act.wait_ge(rstd_ready, q + 1)
                for t in range(MT):
                    nc.scalar.activation(nat[:, q % 2, t4(t)], src[:, t4(t)], ACT.Identity, bias=shift[:, t:t + 1],
                                         scale=rstd[:, t:t + 1]).then_inc(nat_ready, 1)

            split_hi(0)
            for kind, i in order:
                if kind == "cur":
                    if i + 1 < len(blocks):
                        split_hi(i + 1)
                    bl = blocks[i]
                    if bl["s"] == 0 and i == steps[bl["g"]]["first"]:
                        if bl["g"] == 0:
                            act.wait_ge(xt_in, 16)
                            act.wait_ge(alpha_ready, 1)
                        nc.scalar.activation(vt[:, 0, col(bl["n"])], vt[:, 0, col(bl["n"])], ACT.Copy,
                                             scale=al[:, 1:2]).then_inc(x_scaled, 1)
                    continue
                if kind == "next":
                    continue
                g = i
                s, n = steps[g]["s"], steps[g]["n"]
                q = ln_index(g)
                if kind in ("w", "out"):
                    deviation(q)
                elif kind == "norm" and s == 0:
                    if q >= 2:
                        act.wait_ge(turned, q - 1)
                        act.wait_ge(v_lo_ready, q - 1)
                    normalise(q, pre)
                    act.wait_ge(nat_ready, MT * (q + 1))
                    nc.scalar.activation(v_hi[:, 1, col(n)], nat[:, q % 2, :], ACT.Copy).then_inc(v_hi_ready, 1)
                elif kind == "norm":
                    if g >= FINAL + 2:
                        act.wait_ge(stored[q % 2], 16 * ((g - FINAL) // 2))
                    else:
                        act.wait_ge(v_lo_ready, NB)
                    normalise(q, p_rows)
                elif kind == "turn" and s == 0:
                    act.wait_ge(turned, g + 1)
                    nc.scalar.copy(vt[:, 1, col(n)], p_turn[:]).then_inc(vt_copied, 1)
                elif kind == "turn":
                    act.wait_ge(turned, g + 1)
                    nc.scalar.activation(v_hi[:, (s + 1) % 2, col(n)], p_turn[:], ACT.Copy).then_inc(v_hi_ready, 1)

        @block.vector
        def _(dve):
            chain = [0]

            def link(ins):
                chain[0] += 1
                ins.then_inc(dve_chain, 1)
                dve.wait_ge(dve_chain, chain[0])

            nc.vector.memset(eps[:], EPS).then_inc(eps_ready, 1)

            def split_lo(i):
                bl = blocks[i]
                if i < NB:
                    dve.wait_ge(x_hi_ready, i + 1)
                    nc.vector.tensor_tensor(v_lo[:, 0, col(i)], yt[:, col(i)], v_hi[:, 0, col(i)].bitcast(F32),
                                            ALU.subtract).then_inc(x_lo_ready, 1)
                dve.wait_ge(hi_ready, i + 1)
                dve.wait_ge(raw_in[i % RAW_SLOTS], 16 * (i // RAW_SLOTS + 1))
                if bl["s"] == 0:
                    k = bl["g"]
                    acc = sum_dve[:, k % 2, :]
                    for t in range(pool_tiles(i), MT):
                        a = raw[:, i % RAW_SLOTS, t * BLK:(t + 1) * BLK]
                        if i == steps[k]["first"]:
                            if k >= 2:
                                dve.wait_ge(w_done, k - 1)
                            link(nc.vector.tensor_copy(acc, a))
                        else:
                            link(nc.vector.tensor_tensor(acc, acc, a, ALU.add))
                if i >= SPLIT_SLOTS:
                    dve.wait_ge(block_used, i - SPLIT_SLOTS + 1)
                nc.vector.tensor_tensor(a_lo[:, i % SPLIT_SLOTS, :], raw[:, i % RAW_SLOTS, :],
                                        a_hi[:, i % SPLIT_SLOTS, :].bitcast(F32), ALU.subtract).then_inc(lo_ready, 1)

            def join(g):
                s, n = steps[g]["s"], steps[g]["n"]
                if g in part:
                    dve.wait_ge(cur_done, part[g] + 1)
                else:
                    dve.wait_ge(block_used, steps[g]["last"] + 1)
                src = p_cur[g % 2][:]
                dst = vt[:, (s + 1) % 2, col(n)]
                before = made_by.get((s, n))
                if s >= 1 and before in part:
                    dve.wait_ge(part_kept, part[before] + 1)
                if s == 0:
                    dve.wait_ge(x_scaled, g + 1)
                    if g >= 1:
                        dve.wait_ge(w_done, g)
                    ins = nc.vector.scalar_tensor_tensor(out=zt[:], in0=src, scalar=al[:, 0:1], in1=vt[:, 0, col(n)],
                                                         op0=ALU.mult, op1=ALU.add)
                elif s == 1 and before in part:
                    ins = nc.vector.tensor_tensor(dst, src, dst, ALU.add)
                elif s == 1:
                    ins = nc.vector.tensor_copy(dst, src)
                else:
                    ins = nc.vector.scalar_tensor_tensor(out=dst, in0=src, scalar=2.0, in1=dst, op0=ALU.mult,
                                                         op1=ALU.add if before in part else ALU.subtract)
                ins.then_inc(joined, 1)

            def keep_part(g):
                s, n = steps[g]["s"], steps[g]["n"]
                dve.wait_ge(block_used, steps[g]["last"] + 1)
                src, dst = p_next[part[g] % 2][:], vt[:, s % 2, col(n)]
                if s == 0:
                    dve.wait_ge(joined, g + 1)
                    ins = nc.vector.tensor_copy(dst, src)
                else:
                    ins = nc.vector.scalar_tensor_tensor(out=dst, in0=src, scalar=2.0, in1=dst, op0=ALU.mult,
                                                         op1=ALU.subtract)
                ins.then_inc(part_kept, 1)

            def variance(q, src):
                for t in range(MT):
                    ins = nc.vector.bn_stats(stats[:, t, :], src[:, t4(t)])
                link(ins)
                for t in range(MT):
                    ins = nc.vector.bn_aggr(mv[:, t, :], stats[:, t, :])
                ins.then_inc(var_ready, 1)

            def layer0_rows(g):
                n = steps[g]["n"]
                dve.wait_ge(w_done, g + 1)
                if g == 0:
                    dve.wait_ge(b_in, 16)
                if g >= 1:
                    dve.wait_ge(nat_ready, MT * g)
                link(nc.vector.tensor_scalar(deg[:, 0, :], p_deg[:], al[:, 0:1], al[:, 1:2], ALU.mult, ALU.add))
                link(nc.vector.tensor_scalar(deg[:, 1, :], deg[:, 0, :], 0.0, None, ALU.is_equal))
                link(nc.vector.tensor_tensor(deg[:, 2, :], deg[:, 0, :], deg[:, 1, :], ALU.add))
                link(nc.vector.reciprocal(deg[:, 3, :], deg[:, 2, :]))
                link(nc.vector.tensor_tensor(deg[:, 2, :], deg[:, 3, :], deg[:, 1, :], ALU.mult))
                link(nc.vector.tensor_tensor(deg[:, 4, :], deg[:, 3, :], deg[:, 2, :], ALU.subtract))
                for t in range(MT):
                    ins = nc.vector.scalar_tensor_tensor(out=pre[:, t4(t)], in0=p_rows[:, t4(t)],
                                                         scalar=deg[:, 4, t:t + 1], in1=bb[:], op0=ALU.mult, op1=ALU.add)
                link(ins)
                nc.vector.scalar_tensor_tensor(out=pre[:], in0=pre[:], scalar=0.0, in1=yt[:, col(n)], op0=ALU.max,
                                               op1=ALU.add).then_inc(pre_read, 1)
                dve.wait_ge(pre_read, g + 1)
                variance(g, pre)

            def inverse_deviation(q):
                dve.wait_ge(std_ready, q + 1)
                if q >= 1:
                    dve.wait_ge(nat_ready, MT * q)
                link(nc.vector.reciprocal(rstd[:], std[:]))
                nc.vector.scalar_tensor_tensor(out=shift[:], in0=mv[:, :, 0], scalar=-1.0, in1=rstd[:], op0=ALU.mult,
                                               op1=ALU.mult).then_inc(rstd_ready, 1)

            def split_v_lo(g):
                s, n = steps[g]["s"], steps[g]["n"]
                dve.wait_ge(v_hi_ready, g + 1)
                src = nat[:, g % 2, :] if s == 0 else p_turn[:]
                nc.vector.tensor_tensor(v_lo[:, (s + 1) % 2, col(n)], src,
                                        v_hi[:, (s + 1) % 2, col(n)].bitcast(F32), ALU.subtract).then_inc(v_lo_ready, 1)

            def add_term(g):
                s, n = steps[g]["s"], steps[g]["n"]
                dve.wait_ge(theta_done, g + 1)
                if s >= 1:
                    dve.wait_ge(y_added, made_by[(s, n)] + 1)
                other = vt[:, 1, col(n)] if s == 0 else yt[:, col(n)]
                nc.vector.tensor_tensor(yt[:, col(n)], p_theta[:], other, ALU.add).then_inc(y_added, 1)

            split_lo(0)
            for kind, i in order:
                if kind == "cur":
                    if i + 1 < len(blocks):
                        split_lo(i + 1)
                    if i == 0:
                        dve.wait_ge(al_in, 16)
                        nc.vector.tensor_scalar(al[:, 1:2], al[:, 0:1], -1.0, 1.0, ALU.mult,
                                                ALU.add).then_inc(alpha_ready, 1)
                        dve.wait_ge(alpha_ready, 1)
                    if i == 4:
                        dve.wait_ge(th_in, 16)
                        for k in range(K):
                            ins = nc.vector.tensor_scalar(th[:, k, :], th[:, k, :], COEFF[k], None, ALU.mult)
                        ins.then_inc(theta_ready, 1)
                    g = blocks[i]["g"]
                    if i == steps[g]["last"]:
                        join(g)
                    continue
                if kind == "next":
                    g = blocks[i]["g"]
                    if i == steps[g]["last"]:
                        keep_part(g)
                    continue
                g = i
                if kind == "w":
                    layer0_rows(g)
                elif kind == "out":
                    dve.wait_ge(out_done, g - FINAL + 1)
                    dve.wait_ge(nat_ready, MT * ln_index(g))
                    variance(ln_index(g), p_rows)
                elif kind == "norm":
                    inverse_deviation(ln_index(g))
                elif kind == "turn":
                    split_v_lo(g)
                elif kind == "theta":
                    add_term(g)

        @block.tensor
        def _(pe):
            def use_block(i, ahead):
                bl = blocks[i]
                g, m = bl["g"], bl["m"]
                st = steps[g]
                j = bl["s"] + ahead
                if ahead:
                    bank = p_next[part[g] % 2]
                    starts, ends = i == st["first"] + st["once"], i == st["last"]
                    if starts and part[g] >= 2:
                        pe.wait_ge(part_kept, part[g] - 1)
                else:
                    bank = p_cur[g % 2]
                    starts, ends = i == st["first"], i == st["last"]
                    if starts and g >= 2:
                        pe.wait_ge(joined, g - 1)
                    pe.wait_ge(hi_ready, i + 1)
                    pe.wait_ge(lo_ready, i + 1)
                if j == 0:
                    if g == 0:
                        pe.wait_ge(x_hi_ready, m + 1)
                        pe.wait_ge(x_lo_ready, m + 1)
                else:
                    pe.wait_ge(v_hi_ready, made_by[(j, m)] + 1)
                    pe.wait_ge(v_lo_ready, made_by[(j, m)] + 1)
                for t in range(MT):
                    hi = a_hi[:, i % SPLIT_SLOTS, t * BLK:(t + 1) * BLK]
                    lo = a_lo[:, i % SPLIT_SLOTS, t * BLK:(t + 1) * BLK]
                    vh, vl = v_hi[:, j % 2, tile(m, t)], v_lo[:, j % 2, tile(m, t)]
                    first, last = starts and t == 0, ends and t == MT - 1
                    nc.tensor.matmul(bank[:], vh, hi, start=first, stop=False)
                    nc.tensor.matmul(bank[:], vh, lo, start=False, stop=False)
                    ins = nc.tensor.matmul(bank[:], vl, hi, start=False, stop=last)
                if ahead or not bl["twice"]:
                    ins.then_inc(block_used, 1)
                elif ends:
                    ins.then_inc(cur_done, 1)

            def project(g):
                if g == 0:
                    pe.wait_ge(w_in, 16)
                    pe.wait_ge(consts_ready, 1)
                pe.wait_ge(joined, g + 1)
                if g >= 1:
                    pe.wait_ge(pre_read, g)
                pe.wait_ge(pool_summed, steps[g]["last"] + 1)
                for t in range(MT):
                    nc.tensor.matmul(p_rows[:, t4(t)], zt[:, t4(t)], wt[:], start=True, stop=True)
                for t in range(MT):
                    nc.tensor.matmul(p_deg[:, t:t + 1], sum_pool[:, g % 2, t4(t)], ones[:], start=True, stop=False)
                    ins = nc.tensor.matmul(p_deg[:, t:t + 1], sum_dve[:, g % 2, t4(t)], ones[:], start=False, stop=True)
                ins.then_inc(w_done, 1)

            def turn(g):
                s, n = steps[g]["s"], steps[g]["n"]
                if s == 0:
                    pe.wait_ge(nat_ready, MT * (g + 1))
                    if g >= 1:
                        pe.wait_ge(vt_copied, g)
                else:
                    pe.wait_ge(joined, g + 1)
                    if g == NB:
                        pe.wait_ge(vt_copied, NB)
                    else:
                        pe.wait_ge(v_lo_ready, g)
                for t in range(MT):
                    src = nat[:, g % 2, t4(t)] if s == 0 else vt[:, (s + 1) % 2, tile(n, t)]
                    ins = nc.tensor.transpose(p_turn[:, t4(t)], src, ident[:])
                ins.then_inc(turned, 1)

            def term(g):
                s, n = steps[g]["s"], steps[g]["n"]
                if g == 0:
                    pe.wait_ge(theta_ready, 1)
                if s == 0:
                    pe.wait_ge(vt_copied, g + 1)
                if g >= 1:
                    pe.wait_ge(y_added, g)
                nc.tensor.matmul(p_theta[:], th[:, s, :], vt[:, (s + 1) % 2, col(n)], start=True,
                                 stop=True).then_inc(theta_done, 1)

            def output_rows(g):
                s, n = steps[g]["s"], steps[g]["n"]
                pe.wait_ge(joined, g + 1)
                pe.wait_ge(y_added, FINAL)
                if g == FINAL:
                    pe.wait_ge(pre_read, NB)
                pe.wait_ge(nat_ready, MT * ln_index(g))
                for t in range(MT):
                    nc.tensor.matmul(p_rows[:, t4(t)], yt[:, tile(n, t)], ident[:], start=True, stop=False)
                    ins = nc.tensor.matmul(p_rows[:, t4(t)], vt[:, (s + 1) % 2, tile(n, t)], th[:, K - 1, :],
                                           start=False, stop=True)
                ins.then_inc(out_done, 1)

            for kind, i in order:
                if kind == "cur":
                    use_block(i, 0)
                elif kind == "next":
                    use_block(i, 1)
                elif kind == "w":
                    project(i)
                elif kind == "turn":
                    turn(i)
                elif kind == "theta":
                    term(i)
                elif kind == "out":
                    output_rows(i)


def kernel(x, adj, L0_gnn_t, L0_gnn_alpha, L0_gnn_W, L0_gnn_b, L1_gnn_theta):
    import concourse.bacc as bacc
    from concourse.bass_utils import run_bass_kernel_spmd

    x, adj, w, theta = (np.asarray(v) for v in (x, adj, L0_gnn_W, L1_gnn_theta))
    arrays = {
        "a_blocks": np.ascontiguousarray(adj.reshape(NB, BLK, NB, MT, P).transpose(0, 2, 4, 3, 1)).reshape(NB, NB, P, MT * BLK),
        "x_nat": np.ascontiguousarray(x.reshape(NB, MT, P, P).transpose(0, 2, 1, 3)).reshape(NB, P, BLK),
        "x_t": np.ascontiguousarray(x.T),
        "alpha": np.asarray(L0_gnn_alpha).reshape(1, 1),
        "w_t": np.ascontiguousarray(w.T),
        "b": np.asarray(L0_gnn_b).reshape(1, P),
        "theta": np.ascontiguousarray(theta.transpose(1, 0, 2)),
    }
    nc = bacc.Bacc("TRN2", target_bir_lowering=False, num_devices=1)
    args = [nc.dram_tensor(name, a.shape, mybir.dt.from_np(a.dtype), kind="ExternalInput").ap()
            for name, a in arrays.items()]
    out = nc.dram_tensor("out", (NB, MT, P, P), F32, kind="ExternalOutput").ap()
    graph_layers(nc, *args, out.rearrange("n t p f -> n p t f"))
    r = run_bass_kernel_spmd(nc, [arrays], core_ids=[0])
    return r.results[0]["out"].reshape(N, P)
```

```python
from contextlib import ExitStack

import numpy as np

import concourse.bass as bass
from concourse import mybir

ALU = mybir.AluOpType
ACT = mybir.ActivationFunctionType
F32 = mybir.dt.float32
F32R = mybir.dt.float32r

P = 128
N = 4096
BLK = 512
NB = N // BLK
MT = BLK // P
K = 5
SWEEPS = K
PT = 2
PPB = MT // PT
PW = PT * BLK
RAW_SLOTS = 5
SPLIT_SLOTS = 7
LAG = 2
AHEAD = SPLIT_SLOTS - 1 - LAG
EPS = 1e-5
TAU = 0.5
COEFF = [float(2.0 / K * np.exp(-TAU * np.cos(np.pi * (k + 0.5) / K))) for k in range(K)]


def plan_pieces():
    blocks, steps = [], []
    for s in range(SWEEPS):
        rows = range(NB) if s % 2 == 0 else range(NB - 1, -1, -1)
        for n in rows:
            g = len(steps)
            before = list(range(n)) if s % 2 == 0 else list(range(NB - 1, n, -1))
            twice = s < SWEEPS - 1 and bool(before)
            steps.append(dict(s=s, g=g, n=n, twice=twice))
            if s == 0:
                once, due = list(range(n, NB)), list(before)
                for q in range(NB):
                    if (q + 1) * n // NB > n - len(due):
                        blocks.append((g, n, due.pop(0), True))
                    else:
                        blocks.append((g, n, once.pop(0), False))
            else:
                blocks.append((g, n, n, False))
                if g % NB == 1:
                    blocks[-2], blocks[-1] = blocks[-1], blocks[-2]
                blocks += [(g, n, m, twice) for m in before]
    pieces = [dict(s=steps[g]["s"], g=g, n=n, m=m, part=q, twice=twice)
              for g, n, m, twice in blocks for q in range(PPB)]
    for h, pc in enumerate(pieces):
        st = steps[pc["g"]]
        pc["cur_starts"] = "first" not in st
        st.setdefault("first", h)
        st["last"] = h
        if pc["twice"]:
            pc["next_starts"] = "next_first" not in st
            st.setdefault("next_first", h)
            st["next_last"] = h
    return pieces, steps


def plan_order(pieces, steps):
    made_by = {(st["s"] + 1, st["n"]): st["g"] for st in steps}
    order, closing, lagging = [], [], []
    pos = 0

    def close(key):
        while closing and ("turn", key) in [it for _, it in closing]:
            order.append(closing.pop(0)[1])

    def emit(kind, h):
        nonlocal pos
        pc = pieces[h]
        j = pc["s"] + (kind == "next")
        if j >= 1:
            g = made_by[(j, pc["m"])]
            if kind == "cur" and ("turn", g) in [it for _, it in closing]:
                while lagging:
                    emit("next", lagging.pop(0))
            close(g)
        while closing and closing[0][0] <= pos:
            order.append(closing.pop(0)[1])
        order.append((kind, h))
        pos += 1
        if kind == "cur" and h == steps[pc["g"]]["last"]:
            g = pc["g"]
            stages = CLOSING[0 if pc["s"] == 0 else 2 if pc["s"] == SWEEPS - 1 else 1]
            closing.extend((pos + d, (stage, g)) for d, stage in stages)

    for h, pc in enumerate(pieces):
        emit("cur", h)
        if pc["twice"]:
            lagging.append(h)
        while lagging and lagging[0] <= h - LAG:
            emit("next", lagging.pop(0))
    order += [it for _, it in closing]
    return order


CLOSING = [
    [(0, "deg"), (4, "w"), (6, "dev"), (7, "rstd"), (11, "norm"), (15, "turn"), (20, "theta")],
    [(2, "turn"), (3, "theta")],
    [(3, "out"), (5, "dev"), (5, "rstd"), (8, "norm")],
]


def graph_layers(nc, a_pieces, x_nat, x_t, alpha, w_t, b, theta, out):
    pieces, steps = plan_pieces()
    order = plan_order(pieces, steps)
    made_by = {(st["s"] + 1, st["n"]): st["g"] for st in steps}
    part = {st["g"]: q for q, st in enumerate(x for x in steps if x["twice"])}
    sweep0 = [h for h, pc in enumerate(pieces) if pc["s"] == 0]
    released = {}
    for kind, h in order:
        if kind == "next" or kind == "cur" and not pieces[h]["twice"]:
            released[h] = len(released) + 1
    FINAL = (SWEEPS - 1) * NB

    with ExitStack() as ctx:
        def sb(name, shape, dt=F32):
            return ctx.enter_context(nc.sbuf_tensor(name, shape, dt))

        def ps(name, shape):
            return ctx.enter_context(nc.psum_tensor(name, shape, F32))

        def sem(name):
            return ctx.enter_context(nc.semaphore(name))

        raw = sb("raw", [P, RAW_SLOTS, PW])
        a_hi = sb("a_hi", [P, SPLIT_SLOTS, PW], F32R)
        a_lo = sb("a_lo", [P, SPLIT_SLOTS, PW], F32R)
        v_hi = sb("v_hi", [P, 2, N], F32R)
        v_lo = sb("v_lo", [P, 2, N], F32R)
        vt = sb("vt", [P, 2, N])
        yt = sb("yt", [P, N])
        th = sb("th", [P, K, P])
        wt = sb("wt", [P, P])
        bb = sb("bb", [P, P])
        al = sb("al", [P, 2])
        ident = sb("ident", [P, P])
        ones = sb("ones", [P, 1])
        eps = sb("eps", [P, 1])
        sum_pool = sb("sum_pool", [P, 2, BLK])
        sum_dve = sb("sum_dve", [P, 2, BLK])
        zt = sb("zt", [P, BLK])
        nat = sb("nat", [P, 2, BLK])
        deg = sb("deg", [P, 5, MT])
        stats = sb("stats", [P, MT, 6])
        mv = sb("mv", [P, MT, 2])
        std = sb("std", [P, MT])
        rstd = sb("rstd", [P, MT])
        shift = sb("shift", [P, MT])

        p_cur = [ps(f"p_cur{q}", [P, BLK]) for q in range(2)]
        p_next = [ps(f"p_next{q}", [P, BLK]) for q in range(2)]
        p_turn = ps("p_turn", [P, BLK])
        p_theta = ps("p_theta", [P, BLK])
        p_rows = ps("p_rows", [P, BLK])
        p_deg = ps("p_deg", [P, MT])

        raw_in = [sem(f"raw_in{q}") for q in range(RAW_SLOTS)]
        x_in = [sem(f"x_in{c}") for c in range(NB)]
        xt_in = [sem(f"xt_in{c}") for c in range(NB)]
        al_in, w_in, b_in, th_in = sem("al_in"), sem("w_in"), sem("b_in"), sem("th_in")
        alpha_ready, consts_ready, eps_ready = sem("alpha_ready"), sem("consts_ready"), sem("eps_ready")
        theta_ready = sem("theta_ready")
        x_hi_ready, x_lo_ready, x_scaled = sem("x_hi_ready"), sem("x_lo_ready"), sem("x_scaled")
        hi_ready, lo_ready = sem("hi_ready"), sem("lo_ready")
        pool_summed, pool_chain = sem("pool_summed"), sem("pool_chain")
        dve_chain = sem("dve_chain")
        piece_used = sem("piece_used")
        cur_done = sem("cur_done")
        joined = sem("joined")
        part_kept = sem("part_kept")
        w_done, deg_done = sem("w_done"), sem("deg_done")
        inv_ready, pre_ready = sem("inv_ready"), sem("pre_ready")
        var_ready, std_ready, rstd_ready, nat_ready = (
            sem("var_ready"), sem("std_ready"), sem("rstd_ready"), sem("nat_ready"))
        turned, vt_copied = sem("turned"), sem("vt_copied")
        v_hi_ready, v_lo_ready = sem("v_hi_ready"), sem("v_lo_ready")
        theta_done, y_added = sem("theta_done"), sem("y_added")
        out_done, stored = sem("out_done"), [sem(f"stored{q}") for q in range(2)]

        def col(n):
            return slice(n * BLK, (n + 1) * BLK)

        def tile(n, t):
            return slice(n * BLK + t * P, n * BLK + (t + 1) * P)

        def feat(t):
            return slice(t * P, (t + 1) * P)

        def pool_tiles(h):
            return PT if pieces[h]["part"] == 0 else PT - 1

        def raw_tile(h, t):
            return raw[:, h % RAW_SLOTS, t * BLK:(t + 1) * BLK]

        def ln_index(g):
            return g if g < NB else NB + g - FINAL

        block = ctx.enter_context(nc.Block())

        @block.sync
        def _(sp):
            for i, pc in enumerate(pieces):
                if i >= RAW_SLOTS:
                    sp.wait_ge(hi_ready, i - RAW_SLOTS + 1)
                    sp.wait_ge(lo_ready, i - RAW_SLOTS + 1)
                    sp.wait_ge(pool_summed, min(i - RAW_SLOTS + 1, len(sweep0)))
                if pc["g"] == 0 and pc["part"] == 0:
                    sp.dma_start(yt[:, col(pc["m"])], x_nat[pc["m"]]).then_inc(x_in[pc["m"]], 16)
                sp.dma_start(raw[:, i % RAW_SLOTS, :], a_pieces[pc["n"], pc["m"], pc["part"]]).then_inc(raw_in[i % RAW_SLOTS], 16)
                if i == 4:
                    sp.dma_start(al[:, 0:1], alpha.to_broadcast([P, 1])).then_inc(al_in, 16)
                if i == 8:
                    sp.dma_start(wt[:], w_t).then_inc(w_in, 16)
                    sp.dma_start(bb[:], b.to_broadcast([P, P])).then_inc(b_in, 16)
                    sp.dma_start(th[:], theta).then_inc(th_in, 16)
                if pc["s"] == 0 and i == steps[pc["g"]]["first"] + 9:
                    sp.dma_start(vt[:, 0, col(pc["n"])], x_t[pc["n"]]).then_inc(xt_in[pc["n"]], 16)

        @block.gpsimd
        def _(pool):
            chain = [0]

            def link(ins):
                chain[0] += 1
                ins.then_inc(pool_chain, 1)
                pool.wait_ge(pool_chain, chain[0])

            link(nc.gpsimd.memset(ident[:], 0.0))
            link(nc.gpsimd.affine_select(out=ident[:], in_=ident[:], compare_op=ALU.not_equal, fill=1.0, base=0,
                                         pattern=[[-1, P]], channel_multiplier=1))
            nc.gpsimd.memset(ones[:], 1.0).then_inc(consts_ready, 1)

            for h in sweep0:
                k = pieces[h]["g"]
                acc = sum_pool[:, k % 2, :]
                pool.wait_ge(raw_in[h % RAW_SLOTS], 16 * (h // RAW_SLOTS + 1))
                tiles = [raw_tile(h, t) for t in range(pool_tiles(h))]
                if pieces[h]["cur_starts"]:
                    if k >= 2:
                        pool.wait_ge(deg_done, k - 1)
                    nc.gpsimd.tensor_tensor(acc, tiles[0], tiles[1], ALU.add).then_inc(pool_summed, 1)
                else:
                    for a in tiles[:-1]:
                        link(nc.gpsimd.tensor_tensor(acc, acc, a, ALU.add))
                    nc.gpsimd.tensor_tensor(acc, acc, tiles[-1], ALU.add).then_inc(pool_summed, 1)
                pool.wait_ge(pool_summed, h + 1)

            for st in steps[FINAL:]:
                n, q = st["n"], ln_index(st["g"])
                pool.wait_ge(nat_ready, MT * (q + 1))
                pool.dma_start(out[n], nat[:, q % 2, :].rearrange("p (t f) -> p t f", t=MT)).then_inc(stored[q % 2], 16)
            for done in stored:
                pool.wait_ge(done, 16 * NB // 2)

        @block.scalar
        def _(act):

            def split_hi(i):
                pc = pieces[i]
                if pc["g"] == 0 and pc["part"] == 0:
                    m = pc["m"]
                    act.wait_ge(x_in[m], 16)
                    nc.scalar.activation(v_hi[:, 0, col(m)], yt[:, col(m)], ACT.Copy).then_inc(x_hi_ready, 1)
                act.wait_ge(raw_in[i % RAW_SLOTS], 16 * (i // RAW_SLOTS + 1))
                if i >= SPLIT_SLOTS:
                    act.wait_ge(piece_used, released[i - SPLIT_SLOTS])
                nc.scalar.activation(a_hi[:, i % SPLIT_SLOTS, :], raw[:, i % RAW_SLOTS, :], ACT.Copy).then_inc(hi_ready, 1)

            def deviation(q):
                act.wait_ge(var_ready, q + 1)
                if q == 0:
                    act.wait_ge(eps_ready, 1)
                else:
                    act.wait_ge(rstd_ready, q)
                nc.scalar.activation(std[:], mv[:, :, 1], ACT.Sqrt, bias=eps[:]).then_inc(std_ready, 1)

            def normalise(q, src):
                act.wait_ge(rstd_ready, q + 1)
                for t in range(MT):
                    nc.scalar.activation(nat[:, q % 2, feat(t)], src[:, feat(t)], ACT.Identity, bias=shift[:, t:t + 1],
                                         scale=rstd[:, t:t + 1]).then_inc(nat_ready, 1)

            for h in range(AHEAD):
                split_hi(h)
            for kind, i in order:
                if kind == "cur":
                    if i + AHEAD < len(pieces):
                        split_hi(i + AHEAD)
                    pc = pieces[i]
                    if pc["s"] == 0 and i == steps[pc["g"]]["last"] - 4:
                        act.wait_ge(xt_in[pc["n"]], 16)
                        if pc["g"] == 0:
                            act.wait_ge(alpha_ready, 1)
                        nc.scalar.activation(vt[:, 0, col(pc["n"])], vt[:, 0, col(pc["n"])], ACT.Copy,
                                             scale=al[:, 1:2]).then_inc(x_scaled, 1)
                    continue
                if kind == "next":
                    continue
                g = i
                s, n = steps[g]["s"], steps[g]["n"]
                q = ln_index(g)
                if kind == "dev":
                    deviation(q)
                elif kind == "norm" and s == 0:
                    normalise(q, nat[:, q % 2, :])
                    act.wait_ge(nat_ready, MT * (q + 1))
                    nc.scalar.activation(v_hi[:, 1, col(n)], nat[:, q % 2, :], ACT.Copy).then_inc(v_hi_ready, 1)
                elif kind == "norm":
                    if g >= FINAL + 2:
                        act.wait_ge(stored[q % 2], 16 * ((g - FINAL) // 2))
                    else:
                        act.wait_ge(v_lo_ready, NB)
                    normalise(q, p_rows)
                elif kind == "turn" and s == 0:
                    act.wait_ge(turned, g + 1)
                    nc.scalar.copy(vt[:, 1, col(n)], p_turn[:]).then_inc(vt_copied, 1)
                elif kind == "turn":
                    act.wait_ge(turned, g + 1)
                    nc.scalar.activation(v_hi[:, (s + 1) % 2, col(n)], p_turn[:], ACT.Copy).then_inc(v_hi_ready, 1)

        @block.vector
        def _(dve):
            chain = [0]

            def link(ins):
                chain[0] += 1
                ins.then_inc(dve_chain, 1)
                dve.wait_ge(dve_chain, chain[0])

            nc.vector.memset(eps[:], EPS).then_inc(eps_ready, 1)

            def split_lo(i):
                pc = pieces[i]
                if pc["g"] == 0 and pc["part"] == 0:
                    m = pc["m"]
                    dve.wait_ge(x_hi_ready, m + 1)
                    nc.vector.tensor_tensor(v_lo[:, 0, col(m)], yt[:, col(m)], v_hi[:, 0, col(m)].bitcast(F32),
                                            ALU.subtract).then_inc(x_lo_ready, 1)
                dve.wait_ge(raw_in[i % RAW_SLOTS], 16 * (i // RAW_SLOTS + 1))
                if pc["s"] == 0:
                    k = pc["g"]
                    acc = sum_dve[:, k % 2, :]
                    for t in range(pool_tiles(i), PT):
                        if i == steps[k]["first"] + PPB - 1:
                            if k >= 2:
                                dve.wait_ge(deg_done, k - 1)
                            link(nc.vector.tensor_copy(acc, raw_tile(i, t)))
                        else:
                            link(nc.vector.tensor_tensor(acc, acc, raw_tile(i, t), ALU.add))
                dve.wait_ge(hi_ready, i + 1)
                if i >= SPLIT_SLOTS:
                    dve.wait_ge(piece_used, released[i - SPLIT_SLOTS])
                nc.vector.tensor_tensor(a_lo[:, i % SPLIT_SLOTS, :], raw[:, i % RAW_SLOTS, :],
                                        a_hi[:, i % SPLIT_SLOTS, :].bitcast(F32), ALU.subtract).then_inc(lo_ready, 1)

            def join(g):
                s, n = steps[g]["s"], steps[g]["n"]
                if g in part:
                    dve.wait_ge(cur_done, part[g] + 1)
                else:
                    dve.wait_ge(piece_used, released[steps[g]["last"]])
                src = p_cur[g % 2][:]
                dst = vt[:, (s + 1) % 2, col(n)]
                before = made_by.get((s, n))
                if s >= 1 and before in part:
                    dve.wait_ge(part_kept, part[before] + 1)
                if s == 0:
                    dve.wait_ge(x_scaled, g + 1)
                    if g >= 1:
                        dve.wait_ge(w_done, g)
                    ins = nc.vector.scalar_tensor_tensor(out=zt[:], in0=src, scalar=al[:, 0:1], in1=vt[:, 0, col(n)],
                                                         op0=ALU.mult, op1=ALU.add)
                elif s == 1 and before in part:
                    ins = nc.vector.tensor_tensor(dst, src, dst, ALU.add)
                elif s == 1:
                    ins = nc.vector.tensor_copy(dst, src)
                else:
                    ins = nc.vector.scalar_tensor_tensor(out=dst, in0=src, scalar=2.0, in1=dst, op0=ALU.mult,
                                                         op1=ALU.add if before in part else ALU.subtract)
                ins.then_inc(joined, 1)

            def keep_part(g):
                s, n = steps[g]["s"], steps[g]["n"]
                dve.wait_ge(piece_used, released[steps[g]["next_last"]])
                src, dst = p_next[part[g] % 2][:], vt[:, s % 2, col(n)]
                if s == 0:
                    dve.wait_ge(joined, g + 1)
                    ins = nc.vector.tensor_copy(dst, src)
                else:
                    ins = nc.vector.scalar_tensor_tensor(out=dst, in0=src, scalar=2.0, in1=dst, op0=ALU.mult,
                                                         op1=ALU.subtract)
                ins.then_inc(part_kept, 1)

            def variance(q, src):
                for t in range(MT):
                    ins = nc.vector.bn_stats(stats[:, t, :], src[:, feat(t)])
                link(ins)
                for t in range(MT):
                    ins = nc.vector.bn_aggr(mv[:, t, :], stats[:, t, :])
                ins.then_inc(var_ready, 1)

            def inverse_degrees(g):
                dve.wait_ge(deg_done, g + 1)
                link(nc.vector.tensor_scalar(deg[:, 0, :], p_deg[:], al[:, 0:1], al[:, 1:2], ALU.mult, ALU.add))
                link(nc.vector.tensor_scalar(deg[:, 1, :], deg[:, 0, :], 0.0, None, ALU.is_equal))
                link(nc.vector.tensor_tensor(deg[:, 2, :], deg[:, 0, :], deg[:, 1, :], ALU.add))
                link(nc.vector.reciprocal(deg[:, 3, :], deg[:, 2, :]))
                link(nc.vector.tensor_tensor(deg[:, 2, :], deg[:, 3, :], deg[:, 1, :], ALU.mult))
                nc.vector.tensor_tensor(deg[:, 4, :], deg[:, 3, :], deg[:, 2, :], ALU.subtract).then_inc(inv_ready, 1)

            def layer0_rows(g):
                n = steps[g]["n"]
                rows = nat[:, g % 2, :]
                dve.wait_ge(w_done, g + 1)
                dve.wait_ge(inv_ready, g + 1)
                if g == 0:
                    dve.wait_ge(b_in, 16)
                if g >= 1:
                    dve.wait_ge(nat_ready, MT * g)
                if g >= 2:
                    dve.wait_ge(turned, g - 1)
                for t in range(MT):
                    ins = nc.vector.scalar_tensor_tensor(out=rows[:, feat(t)], in0=p_rows[:, feat(t)],
                                                         scalar=deg[:, 4, t:t + 1], in1=bb[:], op0=ALU.mult, op1=ALU.add)
                link(ins)
                nc.vector.scalar_tensor_tensor(out=rows, in0=rows, scalar=0.0, in1=yt[:, col(n)], op0=ALU.max,
                                               op1=ALU.add).then_inc(pre_ready, 1)
                dve.wait_ge(pre_ready, g + 1)
                variance(g, rows)

            def inverse_deviation(q):
                dve.wait_ge(std_ready, q + 1)
                if q >= 1:
                    dve.wait_ge(nat_ready, MT * q)
                link(nc.vector.reciprocal(rstd[:], std[:]))
                nc.vector.scalar_tensor_tensor(out=shift[:], in0=mv[:, :, 0], scalar=-1.0, in1=rstd[:], op0=ALU.mult,
                                               op1=ALU.mult).then_inc(rstd_ready, 1)

            def split_v_lo(g):
                s, n = steps[g]["s"], steps[g]["n"]
                dve.wait_ge(v_hi_ready, g + 1)
                src = nat[:, g % 2, :] if s == 0 else p_turn[:]
                nc.vector.tensor_tensor(v_lo[:, (s + 1) % 2, col(n)], src,
                                        v_hi[:, (s + 1) % 2, col(n)].bitcast(F32), ALU.subtract).then_inc(v_lo_ready, 1)

            def add_term(g):
                s, n = steps[g]["s"], steps[g]["n"]
                dve.wait_ge(theta_done, g + 1)
                if s >= 1:
                    dve.wait_ge(y_added, made_by[(s, n)] + 1)
                other = vt[:, 1, col(n)] if s == 0 else yt[:, col(n)]
                nc.vector.tensor_tensor(yt[:, col(n)], p_theta[:], other, ALU.add).then_inc(y_added, 1)

            for h in range(AHEAD):
                split_lo(h)
            for kind, i in order:
                if kind == "cur":
                    if i + AHEAD < len(pieces):
                        split_lo(i + AHEAD)
                    if i == 0:
                        dve.wait_ge(al_in, 16)
                        nc.vector.tensor_scalar(al[:, 1:2], al[:, 0:1], -1.0, 1.0, ALU.mult,
                                                ALU.add).then_inc(alpha_ready, 1)
                        dve.wait_ge(alpha_ready, 1)
                    if i == 12:
                        dve.wait_ge(th_in, 16)
                        for k in range(K):
                            ins = nc.vector.tensor_scalar(th[:, k, :], th[:, k, :], COEFF[k], None, ALU.mult)
                        ins.then_inc(theta_ready, 1)
                    g = pieces[i]["g"]
                    if i == steps[g]["last"]:
                        join(g)
                    continue
                if kind == "next":
                    g = pieces[i]["g"]
                    if i == steps[g]["next_last"]:
                        keep_part(g)
                    continue
                g = i
                if kind == "deg":
                    inverse_degrees(g)
                elif kind == "w":
                    layer0_rows(g)
                elif kind == "out":
                    dve.wait_ge(out_done, g - FINAL + 1)
                    dve.wait_ge(nat_ready, MT * ln_index(g))
                    variance(ln_index(g), p_rows)
                elif kind == "rstd":
                    inverse_deviation(ln_index(g))
                elif kind == "turn":
                    split_v_lo(g)
                elif kind == "theta":
                    add_term(g)

        @block.tensor
        def _(pe):
            def use_piece(h, ahead):
                pc = pieces[h]
                g, m = pc["g"], pc["m"]
                st = steps[g]
                j = pc["s"] + ahead
                if ahead:
                    bank = p_next[part[g] % 2]
                    starts, ends = pc["next_starts"], h == st["next_last"]
                    if starts and part[g] >= 2:
                        pe.wait_ge(part_kept, part[g] - 1)
                else:
                    bank = p_cur[g % 2]
                    starts, ends = pc["cur_starts"], h == st["last"]
                    if starts and g >= 2:
                        pe.wait_ge(joined, g - 1)
                    pe.wait_ge(hi_ready, h + 1)
                    pe.wait_ge(lo_ready, h + 1)
                if j == 0:
                    if g == 0:
                        pe.wait_ge(x_hi_ready, m + 1)
                        pe.wait_ge(x_lo_ready, m + 1)
                else:
                    pe.wait_ge(v_hi_ready, made_by[(j, m)] + 1)
                    pe.wait_ge(v_lo_ready, made_by[(j, m)] + 1)
                for t in range(PT):
                    hi = a_hi[:, h % SPLIT_SLOTS, t * BLK:(t + 1) * BLK]
                    lo = a_lo[:, h % SPLIT_SLOTS, t * BLK:(t + 1) * BLK]
                    at = tile(m, pc["part"] * PT + t)
                    vh, vl = v_hi[:, j % 2, at], v_lo[:, j % 2, at]
                    nc.tensor.matmul(bank[:], vh, hi, start=starts and t == 0, stop=False)
                    nc.tensor.matmul(bank[:], vh, lo, start=False, stop=False)
                    ins = nc.tensor.matmul(bank[:], vl, hi, start=False, stop=ends and t == PT - 1)
                if ahead or not pc["twice"]:
                    ins.then_inc(piece_used, 1)
                elif ends:
                    ins.then_inc(cur_done, 1)

            def project(g):
                if g == 0:
                    pe.wait_ge(w_in, 16)
                pe.wait_ge(joined, g + 1)
                if g >= 1:
                    pe.wait_ge(pre_ready, g)
                for t in range(MT):
                    ins = nc.tensor.matmul(p_rows[:, feat(t)], zt[:, feat(t)], wt[:], start=True, stop=True)
                ins.then_inc(w_done, 1)

            def degrees(g):
                if g == 0:
                    pe.wait_ge(consts_ready, 1)
                else:
                    pe.wait_ge(inv_ready, g)
                pe.wait_ge(pool_summed, steps[g]["last"] + 1)
                pe.wait_ge(lo_ready, steps[g]["last"] + 1)
                for t in range(MT):
                    nc.tensor.matmul(p_deg[:, t:t + 1], sum_pool[:, g % 2, feat(t)], ones[:], start=True, stop=False)
                    ins = nc.tensor.matmul(p_deg[:, t:t + 1], sum_dve[:, g % 2, feat(t)], ones[:], start=False, stop=True)
                ins.then_inc(deg_done, 1)

            def turn(g):
                s, n = steps[g]["s"], steps[g]["n"]
                if s == 0:
                    pe.wait_ge(nat_ready, MT * (g + 1))
                    if g >= 1:
                        pe.wait_ge(vt_copied, g)
                else:
                    pe.wait_ge(joined, g + 1)
                    if g == NB:
                        pe.wait_ge(vt_copied, NB)
                    else:
                        pe.wait_ge(v_lo_ready, g)
                for t in range(MT):
                    src = nat[:, g % 2, feat(t)] if s == 0 else vt[:, (s + 1) % 2, tile(n, t)]
                    ins = nc.tensor.transpose(p_turn[:, feat(t)], src, ident[:])
                ins.then_inc(turned, 1)

            def term(g):
                s, n = steps[g]["s"], steps[g]["n"]
                if g == 0:
                    pe.wait_ge(theta_ready, 1)
                if s == 0:
                    pe.wait_ge(vt_copied, g + 1)
                if g >= 1:
                    pe.wait_ge(y_added, g)
                nc.tensor.matmul(p_theta[:], th[:, s, :], vt[:, (s + 1) % 2, col(n)], start=True,
                                 stop=True).then_inc(theta_done, 1)

            def output_rows(g):
                s, n = steps[g]["s"], steps[g]["n"]
                pe.wait_ge(joined, g + 1)
                pe.wait_ge(y_added, FINAL)
                if g == FINAL:
                    pe.wait_ge(pre_ready, NB)
                pe.wait_ge(nat_ready, MT * ln_index(g))
                for t in range(MT):
                    nc.tensor.matmul(p_rows[:, feat(t)], yt[:, tile(n, t)], ident[:], start=True, stop=False)
                    ins = nc.tensor.matmul(p_rows[:, feat(t)], vt[:, (s + 1) % 2, tile(n, t)], th[:, K - 1, :],
                                           start=False, stop=True)
                ins.then_inc(out_done, 1)

            for kind, i in order:
                if kind == "cur":
                    use_piece(i, 0)
                elif kind == "next":
                    use_piece(i, 1)
                elif kind == "w":
                    project(i)
                elif kind == "deg":
                    degrees(i)
                elif kind == "turn":
                    turn(i)
                elif kind == "theta":
                    term(i)
                elif kind == "out":
                    output_rows(i)


def kernel(x, adj, L0_gnn_t, L0_gnn_alpha, L0_gnn_W, L0_gnn_b, L1_gnn_theta):
    import concourse.bacc as bacc
    from concourse.bass_utils import run_bass_kernel_spmd

    x, adj, w, theta = (np.asarray(v) for v in (x, adj, L0_gnn_W, L1_gnn_theta))
    arrays = {
        "a_pieces": np.ascontiguousarray(adj.reshape(NB, BLK, NB, PPB, PT, P).transpose(0, 2, 3, 5, 4, 1)).reshape(NB, NB, PPB, P, PW),
        "x_nat": np.ascontiguousarray(x.reshape(NB, MT, P, P).transpose(0, 2, 1, 3)).reshape(NB, P, BLK),
        "x_t": np.ascontiguousarray(x.reshape(NB, BLK, P).transpose(0, 2, 1)),
        "alpha": np.asarray(L0_gnn_alpha).reshape(1, 1),
        "w_t": np.ascontiguousarray(w.T),
        "b": np.asarray(L0_gnn_b).reshape(1, P),
        "theta": np.ascontiguousarray(theta.transpose(1, 0, 2)),
    }
    nc = bacc.Bacc("TRN2", target_bir_lowering=False, num_devices=1)
    args = [nc.dram_tensor(name, a.shape, mybir.dt.from_np(a.dtype), kind="ExternalInput").ap()
            for name, a in arrays.items()]
    out = nc.dram_tensor("out", (NB, MT, P, P), F32, kind="ExternalOutput").ap()
    graph_layers(nc, *args, out.rearrange("n t p f -> n p t f"))
    r = run_bass_kernel_spmd(nc, [arrays], core_ids=[0])
    return r.results[0]["out"].reshape(N, P)
```
